# Optimizing a Trainium2 kernel written in Bass

```python
import numpy as np
import jax
import jax.numpy as jnp

def _softmax(x, axis=-1):
    return jax.nn.softmax(x, axis=axis)

def _gelu(x):
    return jax.nn.gelu(x, approximate=True)

def _silu(x):
    return jax.nn.silu(x)

def _sigmoid(x):
    return jax.nn.sigmoid(x)

def _layernorm(x, axis=-1, eps=1e-05):
    m = jnp.mean(x, axis=axis, keepdims=True)
    v = jnp.var(x, axis=axis, keepdims=True)
    return (x - m) / jnp.sqrt(v + eps)

def _scatter_add(tgt, idx, src, axis=0):
    return tgt.at[idx].add(src)

def _segment_sum(src, seg, n):
    return jax.ops.segment_sum(src, seg, n)
kernel_name = 'mk_rec_standalone_d1_rec_r8_cf7125'

def setup_inputs(seed: int=0):
    np.random.seed(seed)
    _w = jnp.asarray

    def _rec_inputs():
        import jax
        import jax.numpy as jnp
        _rk = jax.random.key(seed)
        r_x = -0.000292821 + 1.00034 * jax.random.normal(jax.random.fold_in(_rk, 1), (2048, 32, 64), jnp.float32)
        return r_x
    r_x = _rec_inputs()

    def _L0_rec_setup():
        import itertools
        import jax, jax.numpy as jnp
        import numpy as np
        N_DIM = 32
        EMB = 64
        PAIRS = np.array(list(itertools.combinations(range(N_DIM), 2)))
        IDX_I = jnp.asarray(PAIRS[:, 0])
        IDX_J = jnp.asarray(PAIRS[:, 1])
        key = jax.random.key(seed)
        k1, k2 = jax.random.split(key)
        x = jax.random.normal(k1, (256, N_DIM, EMB), dtype=jnp.float32)
        W = jax.random.normal(k2, (len(PAIRS), EMB, EMB), dtype=jnp.float32) * (1.0 / np.sqrt(EMB))
        return {'x': x, 'W': W}
    _L0_rec_all = _L0_rec_setup()
    _L0_rec_in = {k: v for k, v in _L0_rec_all.items() if k in ('W',)}
    del _L0_rec_all
    return {'r_x': r_x, 'L0_rec_W': _L0_rec_in['W']}

def reference(r_x, L0_rec_W):
    import jax
    import jax.numpy as jnp

    def _L0_rec_ref(x, W):
        import itertools
        import jax, jax.numpy as jnp
        import numpy as np
        N_DIM = 32
        EMB = 64
        PAIRS = np.array(list(itertools.combinations(range(N_DIM), 2)))
        IDX_I = jnp.asarray(PAIRS[:, 0])
        IDX_J = jnp.asarray(PAIRS[:, 1])
        xi = x[:, IDX_I]
        xj = x[:, IDX_J]
        out = jnp.einsum('bpe,pfe->bpf', xi, W) * xj
        return out
    y = _L0_rec_ref(r_x, L0_rec_W)
    return y

_drawn_inputs = setup_inputs


def setup_inputs(seed=0):
    import zlib

    import numpy as np

    out = dict(_drawn_inputs(seed))
    spreads = {}
    factors = {}
    for name, (base, spread) in spreads.items():
        noise = np.random.default_rng([zlib.crc32(name.encode()), seed]).standard_normal(out[name].shape)
        drawn = base * np.exp(spread * noise) if base else spread * noise
        out[name] = jnp.asarray(drawn.astype(out[name].dtype))
    for name, factor in factors.items():
        out[name] = (out[name] * factor).astype(out[name].dtype)
    return out
```

```python
from contextlib import ExitStack

import concourse.bass as bass
from concourse import mybir

F32 = mybir.dt.float32
ALU = mybir.AluOpType
ACT = mybir.ActivationFunctionType

P = 128
N = 32
E = 64
H = E
M = N // 2
PAIRS = N * (N - 1) // 2
BANK = 512 // E
AREA = 2 * BANK
HIGH = N // 2

CHUNKS = [[0], [1], [2], [3], [4], [5], [6], [7, 8], [9, 10, 11], [12, 13, 14, 15]]
STAGES = 5


def first_pair(i, j):
    return i * (2 * N - i - 1) // 2 + j - i - 1


def weight_col(m):
    return sum(N - 1 - 2 * k for k in range(m))


WCOLS = weight_col(M)
CHUNK_OF = {m: c for c, ms in enumerate(CHUNKS) for m in ms}
CHUNK_AT = [first_pair(2 * ms[0], 2 * ms[0] + 1) for ms in CHUNKS] + [PAIRS]
SLOT = max(b - a for a, b in zip(CHUNK_AT, CHUNK_AT[1:]))


class Step:

    def __init__(self, runs, couple, flip=None, starts=True):
        self.runs = [r for r in runs if r[3] > 0]
        self.chunk = CHUNK_OF[couple]
        self.starts = couple if starts else None
        self.pieces = []
        for m, half, j, n, place in self.runs:
            while n > 0:
                cut = min(n, BANK - place % BANK)
                self.pieces.append((place, half, m, j, cut))
                j, n, place = j + cut, n - cut, place + cut
        self.pieces.sort()
        self.alike = len(self.runs) == 2 and self.runs[0][2:] == self.runs[1][2:]
        self.flip = flip
        self.opens = self.closes = False


def plan():
    steps = []
    for m in range(12):
        i = 2 * m
        if m < HIGH // 2:
            steps.append(Step([(m, 0, HIGH, N - HIGH, 0), (m, 1, HIGH, N - HIGH, 0)], m))
            steps.append(Step([(m, 0, i + 1, HIGH - i - 1, 0), (m, 1, i + 2, HIGH - i - 2, 0)], m,
                              flip=m - 4 if m >= 4 else None, starts=False))
        else:
            steps.append(Step([(m, 0, i + 1, N - i - 1, 0), (m, 1, i + 2, N - i - 2, 0)], m))
    runs = []
    for m, place in ((12, 0), (13, BANK), (14, BANK + 5), (15, BANK - 1)):
        runs.append((m, 0, 2 * m + 1, N - 2 * m - 1, place))
        runs.append((m, 1, 2 * m + 2, N - 2 * m - 2, place))
    steps.append(Step(runs, 12))
    for a, b in zip([None] + steps, steps + [None]):
        if a is None or b is None or a.chunk != b.chunk:
            if b is not None:
                b.opens = True
            if a is not None:
                a.closes = True
    return steps


STEPS = plan()
NSTEP = len(STEPS)
NCHUNK = len(CHUNKS)
FLIPS = 4
WGROUPS = [(0, 1), (1, 2), (2, 4), (4, 8), (8, M)]


def fields_kernel(nc, x, wt, out):
    B = x.shape[0]
    TILES = B // P
    assert TILES % 2 == 0 and TILES >= 4 and NSTEP % 2 == 1 and NCHUNK % STAGES == 0
    x_rows = x.rearrange("b n e -> b (n e)")
    out_rows = out.rearrange("b p f -> b (p f)")

    with ExitStack() as ctx:
        def sb(name, shape):
            return ctx.enter_context(nc.sbuf_tensor(name, shape, F32))

        def sem(name):
            return ctx.enter_context(nc.semaphore(name))

        w_sb = sb("w_sb", [P, WCOLS * E])
        x_sb = [sb(f"x_sb{k}", [P, N * E]) for k in range(2)]
        xT = [sb(f"xT{k}", [P, M, P]) for k in range(2)]
        stage = [sb(f"stage{k}", [P, SLOT * E]) for k in range(STAGES)]
        ones = sb("ones", [P, P])
        ident = sb("ident", [P, P])
        ps = ctx.enter_context(nc.psum_tensor("ps", [P, 2, 2, AREA * E], F32))

        w_in = [sem(f"w_in{g}") for g in range(len(WGROUPS))]
        x_in = [sem(f"x_in{k}") for k in range(2)]
        ones_set = sem("ones_set")
        ident_set = sem("ident_set")
        products = sem("products")
        drained = sem("drained")
        flipped = sem("flipped")
        xT_set = sem("xT_set")
        stored = [sem(f"stored{k}") for k in range(STAGES)]

        block = ctx.enter_context(nc.Block())

        def each_tile(eng, tile):
            tile(0, 0, 0, True, False)
            with eng.Fori(0, TILES // 2 - 1) as i:
                tile(2 * i + 1, i, 1, False, False)
                tile(2 * i + 2, i + 1, 0, False, False)
            tile(TILES - 1, TILES // 2 - 1, 1, False, True)

        def first_bank(g):
            return ps[:, 1, g // 2, (g % 2) * BANK * E:(g % 2 + 1) * BANK * E].rearrange("p (c b) -> p c b", c=4)

        def free_bank(slot):
            return ps[:, slot, 0, BANK * E:2 * BANK * E].rearrange("p (c b) -> p c b", c=4)

        @block.gpsimd
        def _(pool):
            nc.gpsimd.memset(ones[:], 1.0).then_inc(ones_set, 1)
            pool.wait_ge(ones_set, 1)
            nc.gpsimd.affine_select(out=ident[:], in_=ones[:], compare_op=ALU.is_equal, fill=0.0, base=0,
                                    pattern=[[-1, P]], channel_multiplier=1).then_inc(ident_set, 1)

        @block.sync
        def _(sp):
            for g, (a, b) in enumerate(WGROUPS):
                cols = slice(weight_col(a) * E, weight_col(b) * E)
                sp.dma_start(w_sb[:, cols], wt[:, cols]).then_inc(w_in[g], 16)

            def tile(t, times, buf, first, last):
                for k, s in enumerate(STEPS):
                    if s.closes:
                        c = s.chunk
                        a, b = CHUNK_AT[c], CHUNK_AT[c + 1]
                        sp.wait_ge(drained, t * NSTEP + k + 1)
                        sp.dma_start(out_rows[bass.ds(t * P, P), a * E:b * E],
                                     stage[c % STAGES][:, 0:(b - a) * E]).then_inc(stored[c % STAGES], 16)

            each_tile(sp, tile)
            for k in range(STAGES):
                sp.wait_ge(stored[k], 16 * TILES * (NCHUNK // STAGES))

        @block.scalar
        def _(act):
            act.dma_start(x_sb[0][:, :], x_rows[0:P, :]).then_inc(x_in[0], 16)
            act.dma_start(x_sb[1][:, :], x_rows[P:2 * P, :]).then_inc(x_in[1], 16)
            for g in range(FLIPS):
                act.wait_ge(flipped, g + 1)
                nc.scalar.copy(xT[0][:, 4 * g:4 * g + 4, :], first_bank(g)).then_inc(xT_set, 1)

            def tile(t, times, buf, first, last):
                if last:
                    return
                if not first:
                    act.wait_ge(drained, t * NSTEP)
                    act.dma_start(x_sb[1 - buf][:, :],
                                  x_rows[bass.ds((t + 1) * P, P), :]).then_inc(x_in[1 - buf], 16)
                for k, s in enumerate(STEPS):
                    if s.flip is not None:
                        g = s.flip
                        act.wait_ge(flipped, (t + 1) * FLIPS + g + 1)
                        nc.scalar.copy(xT[1 - buf][:, 4 * g:4 * g + 4, :],
                                       free_bank((k + buf) % 2)).then_inc(xT_set, 1)

            each_tile(act, tile)

        @block.tensor
        def _(pe):
            def flip(g, buf, bank):
                for k in range(4):
                    m = 4 * g + k
                    last = nc.tensor.transpose(bank[:, k, :], x_sb[buf][:, 2 * m * E:2 * (m + 1) * E], ident[:])
                last.then_inc(flipped, 1)

            pe.wait_ge(ident_set, 1)
            pe.wait_ge(x_in[0], 16)
            for g in range(FLIPS):
                flip(g, 0, first_bank(g))

            def tile(t, times, buf, first, last):
                for k, s in enumerate(STEPS):
                    slot = (k + buf) % 2
                    if first:
                        for g, (a, b) in enumerate(WGROUPS):
                            if s.starts == a:
                                pe.wait_ge(w_in[g], 16)
                        if k == 0:
                            pe.wait_ge(xT_set, 1)
                        if k == 1:
                            pe.wait_ge(xT_set, FLIPS)
                    elif k == 0:
                        pe.wait_ge(xT_set, (t + 1) * FLIPS)
                    if not first or k >= 2:
                        pe.wait_ge(drained, t * NSTEP + k - 1)
                    if k >= 2 and STEPS[k - 2].flip is not None and not last:
                        pe.wait_ge(xT_set, (t + 1) * FLIPS + STEPS[k - 2].flip + 1)
                    for place, half, m, j, n in s.pieces:
                        col = (weight_col(m) + j - (2 * m + 1)) * E
                        lanes = slice(half * H, half * H + E)
                        done = nc.tensor.matmul(ps[:, slot, half, place * E:(place + n) * E],
                                                xT[buf][lanes, m, :], w_sb[lanes, col:col + n * E],
                                                start=True, stop=True)
                    done.then_inc(products, 1)
                    if s.flip is not None and not last:
                        if s.flip == 0:
                            pe.wait_ge(x_in[1 - buf], 16 if first else 16 * (times + 1 + buf))
                        flip(s.flip, 1 - buf, free_bank(slot))

            each_tile(pe, tile)

        @block.vector
        def _(dve):
            def both(ap, step, width):
                return bass.AP(ap.tensor, ap.offset, [list(ap.ap[0]), [step, 2], [1, width]])

            def tile(t, times, buf, first, last):
                dve.wait_ge(x_in[buf], 16 * (times + 1))
                for k, s in enumerate(STEPS):
                    slot = (k + buf) % 2
                    st, base = stage[s.chunk % STAGES], CHUNK_AT[s.chunk]
                    if s.opens and not (first and s.chunk < STAGES):
                        dve.wait_ge(stored[s.chunk % STAGES],
                                    16 * (t * (NCHUNK // STAGES) + s.chunk // STAGES))
                    dve.wait_ge(products, t * NSTEP + k + 1)
                    if s.alike:
                        m, _, j, n, place = s.runs[0]
                        a, b = first_pair(2 * m, j) - base, first_pair(2 * m + 1, j) - base
                        done = nc.vector.tensor_tensor(both(st[:, a * E:(a + 1) * E], (b - a) * E, n * E),
                                                       ps[:, slot, :, place * E:(place + n) * E],
                                                       both(x_sb[buf][:, j * E:(j + 1) * E], 0, n * E), ALU.mult)
                    else:
                        for m, half, j, n, place in s.runs:
                            a = first_pair(2 * m + half, j) - base
                            done = nc.vector.tensor_tensor(
                                st[:, a * E:(a + n) * E], ps[:, slot, half, place * E:(place + n) * E],
                                x_sb[buf][:, j * E:(j + n) * E], ALU.mult)
                    done.then_inc(drained, 1)

            each_tile(dve, tile)


def kernel(r_x, L0_rec_W):
    import numpy as np
    import concourse.bacc as bacc
    from concourse.bass_utils import run_bass_kernel_spmd

    x = np.ascontiguousarray(r_x)
    w = np.asarray(L0_rec_W).transpose(2, 0, 1)
    wt = np.zeros((P, WCOLS, E), w.dtype)
    for m in range(M):
        even, odd, end = (first_pair(i, i + 1) for i in (2 * m, 2 * m + 1, 2 * m + 2))
        col = weight_col(m)
        wt[0:E, col:col + odd - even] = w[:, even:odd]
        wt[H:H + E, col + 1:col + 1 + end - odd] = w[:, odd:end]
    wt = wt.reshape(P, WCOLS * E)

    nc = bacc.Bacc("TRN2", target_bir_lowering=False, num_devices=1)
    x_in = nc.dram_tensor("x", x.shape, F32, kind="ExternalInput")
    wt_in = nc.dram_tensor("wt", wt.shape, F32, kind="ExternalInput")
    out = nc.dram_tensor("out", (x.shape[0], PAIRS, E), F32, kind="ExternalOutput")
    fields_kernel(nc, x_in.ap(), wt_in.ap(), out.ap())
    r = run_bass_kernel_spmd(nc, [{"x": x, "wt": wt}], core_ids=[0])
    return r.results[0]["out"]
```

```python
from contextlib import ExitStack

import concourse.bass as bass
from concourse import mybir

F32 = mybir.dt.float32
F32R = mybir.dt.float32r
ALU = mybir.AluOpType

P = 128
N = 32
E = 64
H = E
M = N // 2
PAIRS = N * (N - 1) // 2
BANK = 512 // E
STEP = 2 * BANK
PSLOTS = 3
CHUNKS = 16
CHUNK = PAIRS // CHUNKS
RING = 4
LOOP = RING * CHUNK
BLOCK = 16
BLOCKS = PAIRS // BLOCK
WBUFS = 2
GROUP = 4
GROUPS = N // GROUP
LEFTS = 8
AHEAD = 3


def first_pair(i):
    return i * (2 * N - i - 1) // 2


def plan():
    runs = []
    for i in range(N - 1):
        a, end = first_pair(i), first_pair(i + 1)
        while a < end:
            b = min(end, (a // LOOP + 1) * LOOP)
            parts = -(-(b - a) // STEP)
            size = -(-(b - a) // parts)
            b = min(b, a + size)
            runs.append((i, i + 1 + a - first_pair(i), b - a, a))
            a = b
    steps = []
    for k, r in enumerate(runs):
        rest = len(runs) - k
        joins = steps and sum(q[2] for q in steps[-1]) + r[2] <= STEP and r[3] % LOOP
        if joins and r[2] < BANK and len(steps) + rest > NSTEP:
            steps[-1].append(r)
        else:
            steps.append([r])
    return steps


NSTEP = 45
STEPS = plan()
assert len(STEPS) == NSTEP and NSTEP % PSLOTS == 0 and STEP * 4 > LOOP // 4

STEP_OF = [k for k, s in enumerate(STEPS) for r in s for _ in range(r[2])]
COUPLE_END = [STEP_OF[first_pair(2 * m + 2) - 1 if m < M - 1 else PAIRS - 1] for m in range(M)]
COUPLE_START = [STEP_OF[first_pair(2 * m)] for m in range(M)]


def flip_plan():
    plan, at = {}, -1
    for m in list(range(4, M)) + list(range(M, M + 4)):
        at += 2 if m < LEFTS else 1
        if m >= LEFTS:
            at = max(at, COUPLE_END[m - LEFTS] + 1)
        assert at < (NSTEP if m >= M else COUPLE_START[m] - 1)
        plan[at] = (m % M, m >= M)
    return plan


FLIPS = flip_plan()


def fields_kernel(nc, x, w, out):
    TILES = x.shape[0] // P
    assert TILES % 2 == 0 and TILES >= 4
    x_rows = x.rearrange("b n e -> b (n e)")
    out_rows = out.rearrange("b p f -> b (p f)")
    w_blocks = w.rearrange("k e n -> (k e) n")

    with ExitStack() as ctx:
        def sb(name, shape, dt=F32):
            return ctx.enter_context(nc.sbuf_tensor(name, shape, dt))

        def sem(name):
            return ctx.enter_context(nc.semaphore(name))

        w_parts = sb("w_parts", [P, PAIRS * E], F32R)
        w_raw = [sb(f"w_raw{k}", [P, BLOCK * E]) for k in range(WBUFS)]
        x_sb = [sb(f"x_sb{k}", [P, N * E]) for k in range(2)]
        x_high = [sb(f"x_high{k}", [P, GROUP * 2 * E], F32R) for k in range(2)]
        x_low = [sb(f"x_low{k}", [P, GROUP * 2 * E]) for k in range(2)]
        left = sb("left", [P, LEFTS, 4, P], F32R)
        staging = sb("staging", [P, LOOP * E])
        ident = sb("ident", [P, P])
        products = [ctx.enter_context(nc.psum_tensor(f"products{k}", [P, STEP * E], F32)) for k in range(PSLOTS)]
        flip_bank = [ctx.enter_context(nc.psum_tensor(f"flip_bank{k}", [P, 4, P], F32)) for k in range(2)]

        w_in = [sem(f"w_in{k}") for k in range(WBUFS)]
        w_high_set = sem("w_high_set")
        w_low_set = sem("w_low_set")
        x0_in = [sem(f"x0_in{k}") for k in range(2)]
        x_in = [sem(f"x_in{k}") for k in range(2)]
        ones_set = sem("ones_set")
        ident_set = sem("ident_set")
        x_high_set = sem("x_high_set")
        x_low_set = sem("x_low_set")
        flipped = sem("flipped")
        left_set = sem("left_set")
        multiplied = sem("multiplied")
        drained = sem("drained")
        stored = [sem(f"stored{k}") for k in range(RING)]

        block = ctx.enter_context(nc.Block())

        def each_tile(eng, tile):
            tile(0, 0, 0, True, False)
            with eng.Fori(0, TILES // 2 - 1) as i:
                tile(2 * i + 1, i, 1, False, False)
                tile(2 * i + 2, i + 1, 0, False, False)
            tile(TILES - 1, TILES // 2 - 1, 1, False, True)

        def blocks_for(k):
            def reach(k):
                r = STEPS[min(k, NSTEP - 1)][-1]
                return -(-(r[3] + r[2]) // BLOCK)
            return range(0 if k == 0 else reach(k - 1 + AHEAD), reach(k + AHEAD))

        def raw(n):
            own = slice(0, H) if n % 2 == 0 else slice(H, P)
            other = slice(H, P) if n % 2 == 0 else slice(0, H)
            return w_raw[n // 2 % WBUFS][own, :], own, other

        def cols(n):
            return slice(n * BLOCK * E, (n + 1) * BLOCK * E)

        def fields(buf, g):
            ap = x_sb[buf][:, g * GROUP * E:(g + 1) * GROUP * E]
            return bass.AP(ap.tensor, ap.offset, [list(ap.ap[0]), [E, GROUP], [0, 2], [1, E]])

        def twice(ap):
            return ap.rearrange("b (n d e) -> b n d e", d=2, e=E)

        def splits(last):
            return [(g, False) for g in range(4, GROUPS)] + [(g, True) for g in range(4) if not last]

        def wait_x(eng, turn, buf, first):
            if first:
                eng.wait_ge(x0_in[0], 16)
                eng.wait_ge(x0_in[1], 16)
            else:
                eng.wait_ge(x_in[buf], 16 * (turn if buf == 0 else turn + 1))

        @block.sync
        def _(sp):
            def load_w(g):
                if g >= WBUFS:
                    sp.wait_ge(w_low_set, 2 * (g - WBUFS + 1))
                n = min(P, BLOCKS * E - g * P)
                sp.dma_start(w_raw[g % WBUFS][0:n, :], w_blocks[g * P:g * P + n, :]).then_inc(w_in[g % WBUFS], 16)

            GW = -(-BLOCKS // 2)
            part = GROUP * E
            sp.dma_start(x_sb[0][:, 0:part], x_rows[0:P, 0:part]).then_inc(x0_in[0], 16)
            load_w(0)
            sp.dma_start(x_sb[0][:, part:N * E], x_rows[0:P, part:N * E]).then_inc(x0_in[1], 16)
            load_w(1)

            def tile(t, turn, buf, first, last):
                for c in range(CHUNKS):
                    if first and c + WBUFS < GW:
                        load_w(c + WBUFS)
                    k = STEP_OF[(c + 1) * CHUNK - 1]
                    sp.wait_ge(drained, t * NSTEP + k + 1)
                    r = c % RING
                    sp.dma_start(out_rows[bass.ds(t * P, P), c * CHUNK * E:(c + 1) * CHUNK * E],
                                 staging[:, r * CHUNK * E:(r + 1) * CHUNK * E]).then_inc(stored[r], 16)
                    if c == 1 and not last:
                        sp.dma_start(x_sb[1 - buf][:, :],
                                     x_rows[bass.ds((t + 1) * P, P), :]).then_inc(x_in[1 - buf], 16)

            each_tile(sp, tile)
            for r in range(RING):
                sp.wait_ge(stored[r], 16 * TILES * (CHUNKS // RING))

        @block.gpsimd
        def _(pool):
            nc.gpsimd.memset(ident[:], 1.0).then_inc(ones_set, 1)
            pool.wait_ge(ones_set, 1)
            nc.gpsimd.affine_select(out=ident[:], in_=ident[:], compare_op=ALU.is_equal, fill=0.0, base=0,
                                    pattern=[[-1, P]], channel_multiplier=1).then_inc(ident_set, 1)

            def low(t, buf, g):
                pool.wait_ge(x_high_set, t * GROUPS + g + 1)
                nc.gpsimd.tensor_tensor(twice(x_low[g % 2][:, :]), fields(buf, g),
                                        twice(x_high[g % 2][:, :].bitcast(F32)), ALU.subtract).then_inc(x_low_set, 1)

            for g in range(4):
                low(0, 0, g)

            def tile(t, turn, buf, first, last):
                for g, following in splits(last):
                    low(t + following, (buf + following) % 2, g)

            each_tile(pool, tile)

        @block.scalar
        def _(act):
            def high(t, buf, g):
                nc.scalar.copy(twice(x_high[g % 2][:, :]), fields(buf, g)).then_inc(x_high_set, 1)

            def copy_left(t, m):
                act.wait_ge(flipped, t * M + m + 1)
                nc.scalar.copy(left[:, m % LEFTS, :, :], flip_bank[m % 2][:, :, :]).then_inc(left_set, 1)

            def w_high(n):
                act.wait_ge(w_in[n // 2 % WBUFS], 16 * (n // 2 // WBUFS + 1))
                src, own, other = raw(n)
                nc.scalar.copy(w_parts[own, cols(n)], src).then_inc(w_high_set, 1)

            act.wait_ge(x0_in[0], 16)
            high(0, 0, 0)
            for n in blocks_for(0):
                if n < 2:
                    w_high(n)
            act.wait_ge(x0_in[1], 16)
            high(0, 0, 1)
            for m in range(4):
                copy_left(0, m)
                if m % 2 == 1:
                    high(0, 0, 2 + m // 2)
            for n in blocks_for(0):
                if n >= 2:
                    w_high(n)

            def tile(t, turn, buf, first, last):
                for k in range(NSTEP):
                    if first and k > 0:
                        for n in blocks_for(k):
                            w_high(n)
                    if k not in FLIPS:
                        continue
                    m, following = FLIPS[k]
                    if following and last:
                        continue
                    copy_left(t + following, m)
                    if m % 2 == 1:
                        g = m // 2 + 2
                        if g < GROUPS:
                            high(t + following, (buf + following) % 2, g)
                        elif g >= GROUPS and not last:
                            if g == GROUPS:
                                wait_x(act, (turn + 1) if buf == 1 else turn, 1 - buf, False)
                            high(t + 1, 1 - buf, g - GROUPS)

            each_tile(act, tile)

        @block.tensor
        def _(pe):
            def flip(t, m, begins=False):
                if m % 2 == 0:
                    pe.wait_ge(x_low_set, t * GROUPS + m // 2 + 1)
                if not (begins and m < 2):
                    pe.wait_ge(left_set, t * M + m - 1)
                g = m // 2
                for q in range(4):
                    part = (x_high if q < 2 else x_low)[g % 2]
                    a = (2 * (m % 2) + q % 2) * 2 * E
                    src = part[:, a:a + 2 * E]
                    done = nc.tensor.transpose(flip_bank[m % 2][:, q, :], src.bitcast(F32) if q < 2 else src, ident[:])
                done.then_inc(flipped, 1)

            pe.wait_ge(ident_set, 1)
            for m in range(4):
                flip(0, m, begins=True)

            def tile(t, turn, buf, first, last):
                couple = -1
                for k, runs in enumerate(STEPS):
                    if first:
                        end = runs[-1][3] + runs[-1][2]
                        pe.wait_ge(w_low_set, -(-end // BLOCK))
                    if not first or k >= PSLOTS:
                        pe.wait_ge(drained, t * NSTEP + k - PSLOTS + 1)
                    if runs[-1][0] // 2 > couple:
                        couple = runs[-1][0] // 2
                        pe.wait_ge(left_set, t * M + couple + 1)
                    place = 0
                    for i, j, n, pair in runs:
                        while n > 0:
                            cut = min(n, BANK - place % BANK)
                            for part in range(2):
                                done = nc.tensor.matmul(products[k % PSLOTS][:, place * E:(place + cut) * E],
                                                        left[:, i // 2 % LEFTS, 2 * part + i % 2, :],
                                                        w_parts[:, pair * E:(pair + cut) * E],
                                                        start=(part == 0), stop=(part == 1))
                            place, pair, n = place + cut, pair + cut, n - cut
                    done.then_inc(multiplied, 1)
                    if k in FLIPS:
                        m, following = FLIPS[k]
                        if not (following and last):
                            flip(t + following, m)

            each_tile(pe, tile)

        @block.vector
        def _(dve):
            def tile(t, turn, buf, first, last):
                wait_x(dve, turn, buf, first)
                fresh = 0
                for k, runs in enumerate(STEPS):
                    if first:
                        for n in blocks_for(k):
                            dve.wait_ge(w_high_set, n + 1)
                            src, own, other = raw(n)
                            nc.vector.tensor_tensor(w_parts[other, cols(n)], src,
                                                    w_parts[own, cols(n)].bitcast(F32),
                                                    ALU.subtract).then_inc(w_low_set, 1)
                    end = runs[-1][3] + runs[-1][2]
                    while fresh * CHUNK < end:
                        if not (first and fresh < RING):
                            dve.wait_ge(stored[fresh % RING], 16 * (t * (CHUNKS // RING) + fresh // RING))
                        fresh += 1
                    dve.wait_ge(multiplied, t * NSTEP + k + 1)
                    place = 0
                    for i, j, n, pair in runs:
                        at = pair % LOOP
                        done = nc.vector.tensor_tensor(staging[:, at * E:(at + n) * E],
                                                       products[k % PSLOTS][:, place * E:(place + n) * E],
                                                       x_sb[buf][:, j * E:(j + n) * E], ALU.mult)
                        place += n
                    done.then_inc(drained, 1)

            each_tile(dve, tile)


def kernel(r_x, L0_rec_W):
    import numpy as np
    import concourse.bacc as bacc
    from concourse.bass_utils import run_bass_kernel_spmd

    x = np.ascontiguousarray(r_x)
    w = np.asarray(L0_rec_W).reshape(BLOCKS, BLOCK, E, E).transpose(0, 3, 1, 2)
    w = np.ascontiguousarray(w.reshape(BLOCKS, E, BLOCK * E))

    nc = bacc.Bacc("TRN2", target_bir_lowering=False, num_devices=1)
    x_in = nc.dram_tensor("x", x.shape, F32, kind="ExternalInput")
    w_in = nc.dram_tensor("w", w.shape, F32, kind="ExternalInput")
    out = nc.dram_tensor("out", (x.shape[0], PAIRS, E), F32, kind="ExternalOutput")
    fields_kernel(nc, x_in.ap(), w_in.ap(), out.ap())
    r = run_bass_kernel_spmd(nc, [{"x": x, "w": w}], core_ids=[0])
    return r.results[0]["out"]
```

```python
from contextlib import ExitStack

import concourse.bass as bass
from concourse import mybir

F32 = mybir.dt.float32
F32R = mybir.dt.float32r
ALU = mybir.AluOpType

P = 128
N = 32
E = 64
H = E
M = N // 2
PAIRS = N * (N - 1) // 2
BANK = 512 // E
STEP = 2 * BANK
PSLOTS = 3
CHUNKS = 16
CHUNK = PAIRS // CHUNKS
RING = 4
LOOP = RING * CHUNK
BLOCK = 16
BLOCKS = PAIRS // BLOCK
WBUFS = 3
GROUP = 4
GROUPS = N // GROUP
LEFTS = 8
AHEAD = 3


def first_pair(i):
    return i * (2 * N - i - 1) // 2


def plan():
    runs = []
    for i in range(N - 1):
        a, end = first_pair(i), first_pair(i + 1)
        while a < end:
            b = min(end, (a // LOOP + 1) * LOOP)
            parts = -(-(b - a) // STEP)
            size = -(-(b - a) // parts)
            b = min(b, a + size)
            runs.append((i, i + 1 + a - first_pair(i), b - a, a))
            a = b
    steps = []
    for k, r in enumerate(runs):
        rest = len(runs) - k
        joins = steps and sum(q[2] for q in steps[-1]) + r[2] <= STEP and r[3] % LOOP
        if joins and r[2] < BANK and len(steps) + rest > NSTEP:
            steps[-1].append(r)
        else:
            steps.append([r])
    return steps


NSTEP = 45
STEPS = plan()
assert len(STEPS) == NSTEP and NSTEP % PSLOTS == 0 and STEP * 4 > LOOP // 4

STEP_OF = [k for k, s in enumerate(STEPS) for r in s for _ in range(r[2])]
COUPLE_END = [STEP_OF[first_pair(2 * m + 2) - 1 if m < M - 1 else PAIRS - 1] for m in range(M)]
COUPLE_START = [STEP_OF[first_pair(2 * m)] for m in range(M)]


def flip_plan():
    plan, at = {}, -1
    for m in list(range(4, M)) + list(range(M, M + 4)):
        at += 2 if m < LEFTS else 1
        if m >= LEFTS:
            at = max(at, COUPLE_END[m - LEFTS] + 1)
        assert at < (NSTEP if m >= M else COUPLE_START[m] - 1)
        plan[at] = (m % M, m >= M)
    return plan


FLIPS = flip_plan()
FIRST_FLIPS = {0: (2, False), 1: (3, False), 2: (4, False), **{k: f for k, f in FLIPS.items() if f != (4, False)}}
assert len(FIRST_FLIPS) == len(FLIPS) + 2


def fields_kernel(nc, x, w, out):
    TILES = x.shape[0] // P
    assert TILES % 2 == 0 and TILES >= 4
    x_rows = x.rearrange("b n e -> b (n e)")
    out_rows = out.rearrange("b p f -> b (p f)")
    w_blocks = w.rearrange("k e n -> (k e) n")

    with ExitStack() as ctx:
        def sb(name, shape, dt=F32):
            return ctx.enter_context(nc.sbuf_tensor(name, shape, dt))

        def sem(name):
            return ctx.enter_context(nc.semaphore(name))

        w_parts = sb("w_parts", [P, PAIRS * E], F32R)
        w_raw = [sb(f"w_raw{k}", [P, BLOCK * E]) for k in range(WBUFS)]
        x_sb = [sb(f"x_sb{k}", [P, N * E]) for k in range(2)]
        x_high = [sb(f"x_high{k}", [P, GROUP * 2 * E], F32R) for k in range(2)]
        x_low = [sb(f"x_low{k}", [P, GROUP * 2 * E]) for k in range(2)]
        left = sb("left", [P, LEFTS, 4, P], F32R)
        staging = sb("staging", [P, LOOP * E])
        ident = sb("ident", [P, P])
        products = [ctx.enter_context(nc.psum_tensor(f"products{k}", [P, STEP * E], F32)) for k in range(PSLOTS)]
        flip_bank = [ctx.enter_context(nc.psum_tensor(f"flip_bank{k}", [P, 4, P], F32)) for k in range(2)]

        first_w_in = [sem(f"first_w_in{k}") for k in range(WBUFS)]
        w_in = [sem(f"w_in{k}") for k in range(WBUFS)]
        w_high_set = sem("w_high_set")
        w_low_set = sem("w_low_set")
        x0_in = [sem(f"x0_in{k}") for k in range(2)]
        x_in = [sem(f"x_in{k}") for k in range(2)]
        ones_set = sem("ones_set")
        ident_set = sem("ident_set")
        x_high_set = sem("x_high_set")
        x_low_set = sem("x_low_set")
        flipped = sem("flipped")
        left_set = sem("left_set")
        multiplied = sem("multiplied")
        drained = sem("drained")
        stored = [sem(f"stored{k}") for k in range(RING)]

        block = ctx.enter_context(nc.Block())

        def each_tile(eng, tile):
            tile(0, 0, 0, True, False)
            with eng.Fori(0, TILES // 2 - 1) as i:
                tile(2 * i + 1, i, 1, False, False)
                tile(2 * i + 2, i + 1, 0, False, False)
            tile(TILES - 1, TILES // 2 - 1, 1, False, True)

        def blocks_for(k):
            def reach(k):
                r = STEPS[min(k + AHEAD, 2 * k + 1, NSTEP - 1)][-1]
                return -(-(r[3] + r[2]) // BLOCK)
            return range(0 if k == 0 else reach(k - 1), reach(k))

        def raw(n):
            own = slice(0, H) if n % 2 == 0 else slice(H, P)
            other = slice(H, P) if n % 2 == 0 else slice(0, H)
            return w_raw[n // 2 % WBUFS][own, :], own, other

        def load_w(eng, g, arrived):
            n = min(P, BLOCKS * E - g * P)
            eng.dma_start(w_raw[g % WBUFS][0:n, :], w_blocks[g * P:g * P + n, :]).then_inc(arrived[g % WBUFS], 16)

        def cols(n):
            return slice(n * BLOCK * E, (n + 1) * BLOCK * E)

        def fields(buf, g):
            ap = x_sb[buf][:, g * GROUP * E:(g + 1) * GROUP * E]
            return bass.AP(ap.tensor, ap.offset, [list(ap.ap[0]), [E, GROUP], [0, 2], [1, E]])

        def twice(ap):
            return ap.rearrange("b (n d e) -> b n d e", d=2, e=E)

        def wait_x(eng, turn, buf, first):
            if first:
                eng.wait_ge(x0_in[0], 16)
                eng.wait_ge(x0_in[1], 16)
            else:
                eng.wait_ge(x_in[buf], 16 * (turn if buf == 0 else turn + 1))

        @block.sync
        def _(sp):
            part = GROUP * E
            sp.dma_start(x_sb[0][:, 0:part], x_rows[0:P, 0:part]).then_inc(x0_in[0], 16)
            load_w(sp, 0, first_w_in)
            sp.dma_start(x_sb[0][:, part:N * E], x_rows[0:P, part:N * E]).then_inc(x0_in[1], 16)
            for g in range(1, WBUFS):
                load_w(sp, g, first_w_in)

            def tile(t, turn, buf, first, last):
                for c in range(CHUNKS):
                    k = STEP_OF[(c + 1) * CHUNK - 1]
                    sp.wait_ge(drained, t * NSTEP + k + 1)
                    r = c % RING
                    sp.dma_start(out_rows[bass.ds(t * P, P), c * CHUNK * E:(c + 1) * CHUNK * E],
                                 staging[:, r * CHUNK * E:(r + 1) * CHUNK * E]).then_inc(stored[r], 16)
                    if c == 1 and not last:
                        sp.dma_start(x_sb[1 - buf][:, :],
                                     x_rows[bass.ds((t + 1) * P, P), :]).then_inc(x_in[1 - buf], 16)

            each_tile(sp, tile)
            for r in range(RING):
                sp.wait_ge(stored[r], 16 * TILES * (CHUNKS // RING))

        @block.gpsimd
        def _(pool):
            nc.gpsimd.memset(ident[:], 1.0).then_inc(ones_set, 1)
            pool.wait_ge(ones_set, 1)
            nc.gpsimd.affine_select(out=ident[:], in_=ident[:], compare_op=ALU.is_equal, fill=0.0, base=0,
                                    pattern=[[-1, P]], channel_multiplier=1).then_inc(ident_set, 1)

            def low(t, buf, g):
                pool.wait_ge(x_high_set, t * GROUPS + g + 1)
                nc.gpsimd.tensor_tensor(twice(x_low[g % 2][:, :]), fields(buf, g),
                                        twice(x_high[g % 2][:, :].bitcast(F32)), ALU.subtract).then_inc(x_low_set, 1)

            for g in range(3):
                low(0, 0, g)

            def tile(t, turn, buf, first, last):
                for k in range(NSTEP):
                    if first:
                        for n in blocks_for(k):
                            if n % 2 == 1 and n // 2 + WBUFS < -(-BLOCKS // 2):
                                pool.wait_ge(w_low_set, n + 1)
                                load_w(nc.gpsimd, n // 2 + WBUFS, w_in)
                    flips = FIRST_FLIPS if first else FLIPS
                    if k in flips:
                        m, following = flips[k]
                        if m % 2 == 1 and not (following and last):
                            g = m // 2 + 2 + following * GROUPS
                            if g < GROUPS or not last:
                                low(t + g // GROUPS, (buf + g // GROUPS) % 2, g % GROUPS)

            each_tile(pool, tile)

        @block.scalar
        def _(act):
            def high(t, buf, g):
                nc.scalar.copy(twice(x_high[g % 2][:, :]), fields(buf, g)).then_inc(x_high_set, 1)

            def copy_left(t, m):
                act.wait_ge(flipped, t * M + m + 1)
                nc.scalar.copy(left[:, m % LEFTS, :, :], flip_bank[m % 2][:, :, :]).then_inc(left_set, 1)

            def w_high(n):
                g = n // 2
                if g < WBUFS:
                    act.wait_ge(first_w_in[g], 16)
                else:
                    act.wait_ge(w_in[g % WBUFS], 16 * (g // WBUFS))
                src, own, other = raw(n)
                nc.scalar.copy(w_parts[own, cols(n)], src).then_inc(w_high_set, 1)

            act.wait_ge(x0_in[0], 16)
            high(0, 0, 0)
            for n in blocks_for(0):
                w_high(n)
            copy_left(0, 0)
            act.wait_ge(x0_in[1], 16)
            high(0, 0, 1)
            copy_left(0, 1)
            high(0, 0, 2)

            def tile(t, turn, buf, first, last):
                for k in range(NSTEP):
                    if first and k > 0:
                        for n in blocks_for(k):
                            w_high(n)
                    flips = FIRST_FLIPS if first else FLIPS
                    if k not in flips:
                        continue
                    m, following = flips[k]
                    if following and last:
                        continue
                    copy_left(t + following, m)
                    if m % 2 == 1:
                        g = m // 2 + 2
                        if g < GROUPS:
                            high(t + following, (buf + following) % 2, g)
                        elif g >= GROUPS and not last:
                            if g == GROUPS:
                                wait_x(act, (turn + 1) if buf == 1 else turn, 1 - buf, False)
                            high(t + 1, 1 - buf, g - GROUPS)

            each_tile(act, tile)

        @block.tensor
        def _(pe):
            def flip(t, m, begins=False):
                if m % 2 == 0:
                    pe.wait_ge(x_low_set, t * GROUPS + m // 2 + 1)
                if not begins:
                    pe.wait_ge(left_set, t * M + m - 1)
                g = m // 2
                for q in range(4):
                    part = (x_high if q < 2 else x_low)[g % 2]
                    a = (2 * (m % 2) + q % 2) * 2 * E
                    src = part[:, a:a + 2 * E]
                    done = nc.tensor.transpose(flip_bank[m % 2][:, q, :], src.bitcast(F32) if q < 2 else src, ident[:])
                done.then_inc(flipped, 1)

            pe.wait_ge(ident_set, 1)
            for m in range(2):
                flip(0, m, begins=True)

            def tile(t, turn, buf, first, last):
                couple = -1
                for k, runs in enumerate(STEPS):
                    if first:
                        end = runs[-1][3] + runs[-1][2]
                        pe.wait_ge(w_low_set, -(-end // BLOCK))
                    if not first or k >= PSLOTS:
                        pe.wait_ge(drained, t * NSTEP + k - PSLOTS + 1)
                    if runs[-1][0] // 2 > couple:
                        couple = runs[-1][0] // 2
                        pe.wait_ge(left_set, t * M + couple + 1)
                    place = 0
                    for i, j, n, pair in runs:
                        while n > 0:
                            cut = min(n, BANK - place % BANK)
                            for part in range(2):
                                done = nc.tensor.matmul(products[k % PSLOTS][:, place * E:(place + cut) * E],
                                                        left[:, i // 2 % LEFTS, 2 * part + i % 2, :],
                                                        w_parts[:, pair * E:(pair + cut) * E],
                                                        start=(part == 0), stop=(part == 1))
                            place, pair, n = place + cut, pair + cut, n - cut
                    done.then_inc(multiplied, 1)
                    flips = FIRST_FLIPS if first else FLIPS
                    if k in flips:
                        m, following = flips[k]
                        if not (following and last):
                            flip(t + following, m)

            each_tile(pe, tile)

        @block.vector
        def _(dve):
            def tile(t, turn, buf, first, last):
                if not first:
                    wait_x(dve, turn, buf, first)
                fresh = 0
                for k, runs in enumerate(STEPS):
                    if first:
                        for n in blocks_for(k):
                            dve.wait_ge(w_high_set, n + 1)
                            src, own, other = raw(n)
                            nc.vector.tensor_tensor(w_parts[other, cols(n)], src,
                                                    w_parts[own, cols(n)].bitcast(F32),
                                                    ALU.subtract).then_inc(w_low_set, 1)
                    if first and k == 0:
                        wait_x(dve, turn, buf, first)
                    end = runs[-1][3] + runs[-1][2]
                    while fresh * CHUNK < end:
                        if not (first and fresh < RING):
                            dve.wait_ge(stored[fresh % RING], 16 * (t * (CHUNKS // RING) + fresh // RING))
                        fresh += 1
                    dve.wait_ge(multiplied, t * NSTEP + k + 1)
                    place = 0
                    for i, j, n, pair in runs:
                        at = pair % LOOP
                        done = nc.vector.tensor_tensor(staging[:, at * E:(at + n) * E],
                                                       products[k % PSLOTS][:, place * E:(place + n) * E],
                                                       x_sb[buf][:, j * E:(j + n) * E], ALU.mult)
                        place += n
                    done.then_inc(drained, 1)

            each_tile(dve, tile)


def kernel(r_x, L0_rec_W):
    import numpy as np
    import concourse.bacc as bacc
    from concourse.bass_utils import run_bass_kernel_spmd

    x = np.ascontiguousarray(r_x)
    w = np.asarray(L0_rec_W).reshape(BLOCKS, BLOCK, E, E).transpose(0, 3, 1, 2)
    w = np.ascontiguousarray(w.reshape(BLOCKS, E, BLOCK * E))

    nc = bacc.Bacc("TRN2", target_bir_lowering=False, num_devices=1)
    x_in = nc.dram_tensor("x", x.shape, F32, kind="ExternalInput")
    w_in = nc.dram_tensor("w", w.shape, F32, kind="ExternalInput")
    out = nc.dram_tensor("out", (x.shape[0], PAIRS, E), F32, kind="ExternalOutput")
    fields_kernel(nc, x_in.ap(), w_in.ap(), out.ap())
    r = run_bass_kernel_spmd(nc, [{"x": x, "w": w}], core_ids=[0])
    return r.results[0]["out"]
```
